# Optimizing a Trainium2 kernel written in Bass

```python
import numpy as np
import jax
import jax.numpy as jnp

def _softmax(x, axis=-1):
    return jax.nn.softmax(x, axis=axis)

def _gelu(x):
    return jax.nn.gelu(x, approximate=True)

def _silu(x):
    return jax.nn.silu(x)

def _sigmoid(x):
    return jax.nn.sigmoid(x)

def _layernorm(x, axis=-1, eps=1e-05):
    m = jnp.mean(x, axis=axis, keepdims=True)
    v = jnp.var(x, axis=axis, keepdims=True)
    return (x - m) / jnp.sqrt(v + eps)

def _scatter_add(tgt, idx, src, axis=0):
    return tgt.at[idx].add(src)

def _segment_sum(src, seg, n):
    return jax.ops.segment_sum(src, seg, n)
kernel_name = 'mk_cond_resid_d1_seqx_r2_3a2dba'

def setup_inputs(seed: int=0):
    np.random.seed(seed)
    _w = jnp.asarray

    def _rec_inputs():
        import jax
        import jax.numpy as jnp
        _rk = jax.random.key(seed)
        x = -7.109e-05 + 0.9999 * jax.random.normal(jax.random.fold_in(_rk, 1), (128, 128, 1024), jnp.float32)
        _lenS = 128 - jax.random.randint(jax.random.fold_in(_rk, 7), (128,), 0, max(1, 128 // 4) + 1, jnp.int32)
        _lenS2 = 128 - jax.random.randint(jax.random.fold_in(_rk, 8), (128,), 0, max(1, 128 // 4) + 1, jnp.int32)
        itok_B_0_7 = jax.random.randint(jax.random.fold_in(_rk, 11), (128,), 0, 8, jnp.int32)
        return (x, itok_B_0_7)
    x, itok_B_0_7 = _rec_inputs()

    def _L0_cond_setup():
        import jax, jax.numpy as jnp
        import numpy as np
        B, C, D, T, N_SUBJECTS = (128, 128, 128, 1024, 8)
        key = jax.random.key(seed)
        kx, ks, kw = jax.random.split(key, 3)
        x = jax.random.normal(kx, (B, C, T), dtype=jnp.float32)
        subjects = jax.random.randint(ks, (B,), 0, N_SUBJECTS, dtype=jnp.int64)
        weights = jax.random.normal(kw, (N_SUBJECTS, C, D), dtype=jnp.float32) * (1.0 / C ** 0.5)
        return {'x': x, 'subjects': subjects, 'weights': weights}
    _L0_cond_all = _L0_cond_setup()
    _L0_cond_in = {k: v for k, v in _L0_cond_all.items() if k in ('weights',)}
    del _L0_cond_all
    return {'x': x, 'itok_B_0_7': itok_B_0_7, 'L0_cond_weights': _L0_cond_in['weights']}

def reference(x, itok_B_0_7, L0_cond_weights):
    import jax
    import jax.numpy as jnp

    def _L0_cond_ref(x, subjects, weights):
        import jax, jax.numpy as jnp
        import numpy as np
        B, C, D, T, N_SUBJECTS = (128, 128, 128, 1024, 8)
        w = weights[subjects]
        out = jnp.einsum('bct,bcd->bdt', x, w)
        return out
    x = x + _L0_cond_ref(x, itok_B_0_7, L0_cond_weights)
    return x

_drawn_inputs = setup_inputs


def setup_inputs(seed=0):
    import zlib

    import numpy as np

    out = dict(_drawn_inputs(seed))
    spreads = {}
    factors = {}
    for name, (base, spread) in spreads.items():
        noise = np.random.default_rng([zlib.crc32(name.encode()), seed]).standard_normal(out[name].shape)
        drawn = base * np.exp(spread * noise) if base else spread * noise
        out[name] = jnp.asarray(drawn.astype(out[name].dtype))
    for name, factor in factors.items():
        out[name] = (out[name] * factor).astype(out[name].dtype)
    return out
```

```python
from contextlib import ExitStack

import concourse.bass as bass
from concourse import mybir

ALU = mybir.AluOpType
F32 = mybir.dt.float32
I32 = mybir.dt.int32

GROUP = 2
SLOTS = 8
BUFS = 4
BANK = 512
DMA = 16


def subject_mix_kernel(nc: bass.Bass, x: bass.AP, subjects: bass.AP, weights: bass.AP, out: bass.AP):
    samples, channels, times = x.shape
    n_subjects, _, mixed = weights.shape
    per_turn = SLOTS * GROUP
    turns = samples // per_turn
    banks = times // BANK
    assert turns * per_turn == samples and banks * BANK == times and channels == mixed == 128
    assert per_turn % BUFS == 0
    uses = per_turn // BUFS

    x_view = x.rearrange("b c t -> c b t")
    out_view = out.rearrange("b d t -> d b t")

    with ExitStack() as ctx:
        def sem(name):
            return ctx.enter_context(nc.semaphore(name))

        ring = ctx.enter_context(nc.sbuf_tensor("ring", [channels, SLOTS, GROUP, times], F32))
        table = ctx.enter_context(nc.sbuf_tensor("table", [channels, n_subjects * mixed], F32))
        subject_row = ctx.enter_context(nc.sbuf_tensor("subject_row", [1, samples], I32))
        selected = ctx.enter_context(nc.sbuf_tensor("selected", [channels, BUFS, mixed], F32))
        products = ctx.enter_context(nc.psum_tensor("products", [mixed, BUFS, times], F32))

        subjects_loaded = sem("subjects_loaded")
        table_loaded = sem("table_loaded")
        x_loaded = [sem(f"x_loaded{s}") for s in range(SLOTS)]
        stored = [sem(f"stored{s}") for s in range(SLOTS)]
        weights_selected = sem("weights_selected")
        product_ready = [sem(f"product_ready{k}") for k in range(BUFS)]
        sum_ready = [sem(f"sum_ready{k}") for k in range(BUFS)]

        block = ctx.enter_context(nc.Block())

        @block.sync
        def _(sp):
            sp.dma_start(subject_row[:], subjects.rearrange("(a b) -> a b", a=1)).then_inc(subjects_loaded, DMA)
            def go_round(turn, first=False):
                for s in range(SLOTS):
                    if not first:
                        sp.wait_ge(stored[s], turn * DMA)
                    start = turn * per_turn + s * GROUP
                    sp.dma_start(ring[:, s], x_view[:, bass.ds(start, GROUP), :]).then_inc(x_loaded[s], DMA)

            go_round(0, first=True)
            with sp.Fori(1, turns) as turn:
                go_round(turn)

        @block.gpsimd
        def _(pool):
            pool.wait_ge(subjects_loaded, DMA)
            pool.wait_ge(table_loaded, DMA)
            def go_round(turn, first=False):
                for j in range(per_turn):
                    k = j % BUFS
                    subject = pool.value_load(subject_row[0:1, bass.ds(turn * per_turn + j, 1)],
                                              min_val=0, max_val=n_subjects - 1)
                    if not first or j >= BUFS:
                        pool.wait_ge(product_ready[k], turn * uses + j // BUFS)
                    nc.gpsimd.tensor_copy(selected[:, k, :],
                                          table[:, bass.ds(subject * mixed, mixed)]).then_inc(weights_selected, 1)

            go_round(0, first=True)
            with pool.Fori(1, turns) as turn:
                go_round(turn)

        @block.tensor
        def _(pe):
            def go_round(turn, first=False):
                for j in range(per_turn):
                    s, g, k = j // GROUP, j % GROUP, j % BUFS
                    if g == 0:
                        pe.wait_ge(x_loaded[s], turn * DMA + DMA)
                    pe.wait_ge(weights_selected, turn * per_turn + j + 1)
                    if not first or j >= BUFS:
                        pe.wait_ge(sum_ready[k], turn * uses + j // BUFS)
                    for n in range(banks):
                        cols = slice(n * BANK, (n + 1) * BANK)
                        product = nc.tensor.matmul(products[:, k, cols], selected[:, k, :], ring[:, s, g, cols],
                                                   start=True, stop=True)
                    product.then_inc(product_ready[k], 1)

            go_round(0, first=True)
            with pe.Fori(1, turns) as turn:
                go_round(turn)

        @block.vector
        def _(dve):
            def go_round(turn, first=False):
                for j in range(per_turn):
                    s, g, k = j // GROUP, j % GROUP, j % BUFS
                    dve.wait_ge(product_ready[k], turn * uses + j // BUFS + 1)
                    nc.vector.tensor_tensor(ring[:, s, g, :], products[:, k, :], ring[:, s, g, :],
                                            ALU.add).then_inc(sum_ready[k], 1)

            go_round(0, first=True)
            with dve.Fori(1, turns) as turn:
                go_round(turn)

        @block.scalar
        def _(act):
            act.dma_start(table[:].rearrange("c (n d) -> c n d", n=n_subjects),
                          weights.rearrange("n c d -> c n d")).then_inc(table_loaded, DMA)
            def go_round(turn, first=False):
                for s in range(SLOTS):
                    start = turn * per_turn + s * GROUP
                    for j in range(s * GROUP, (s + 1) * GROUP):
                        act.wait_ge(sum_ready[j % BUFS], turn * uses + j // BUFS + 1)
                    act.dma_start(out_view[:, bass.ds(start, GROUP), :], ring[:, s]).then_inc(stored[s], DMA)

            go_round(0, first=True)
            with act.Fori(1, turns) as turn:
                go_round(turn)
            for s in range(SLOTS):
                act.wait_ge(stored[s], turns * DMA)


def kernel(x, itok_B_0_7, L0_cond_weights):
    import numpy as np
    import concourse.bacc as bacc
    from concourse.bass_utils import run_bass_kernel_spmd

    nc = bacc.Bacc("TRN2", target_bir_lowering=False, num_devices=1)
    inputs = {"x": np.ascontiguousarray(x), "subjects": np.ascontiguousarray(itok_B_0_7),
              "weights": np.ascontiguousarray(L0_cond_weights)}
    handles = [nc.dram_tensor(name, a.shape, mybir.dt.from_np(a.dtype), kind="ExternalInput").ap()
               for name, a in inputs.items()]
    out = nc.dram_tensor("out", inputs["x"].shape, F32, kind="ExternalOutput").ap()
    subject_mix_kernel(nc, *handles, out)
    result = run_bass_kernel_spmd(nc, [inputs], core_ids=[0])
    return result.results[0]["out"]
```

```python
from contextlib import ExitStack

import concourse.bass as bass
from concourse import mybir

ALU = mybir.AluOpType
F32 = mybir.dt.float32
I32 = mybir.dt.int32

GROUP = 2
SLOTS = 8
BUFS = 4
BANK = 512
DMA = 16


def subject_mix_kernel(nc: bass.Bass, x: bass.AP, subjects: bass.AP, weights: bass.AP, out: bass.AP):
    samples, channels, times = x.shape
    n_subjects, _, mixed = weights.shape
    per_turn = SLOTS * GROUP
    turns = samples // per_turn
    banks = times // BANK
    assert turns * per_turn == samples and banks * BANK == times and channels == mixed == 128
    assert per_turn % BUFS == 0
    uses = per_turn // BUFS

    x_view = x.rearrange("b c t -> c b t")
    out_view = out.rearrange("b d t -> d b t")

    with ExitStack() as ctx:
        def sem(name):
            return ctx.enter_context(nc.semaphore(name))

        ring = ctx.enter_context(nc.sbuf_tensor("ring", [channels, SLOTS, GROUP, times], F32))
        table = ctx.enter_context(nc.sbuf_tensor("table", [channels, n_subjects * mixed], F32))
        subject_row = ctx.enter_context(nc.sbuf_tensor("subject_row", [1, samples], I32))
        selected = ctx.enter_context(nc.sbuf_tensor("selected", [channels, BUFS, mixed], F32))
        products = ctx.enter_context(nc.psum_tensor("products", [mixed, BUFS, times], F32))

        subjects_loaded = sem("subjects_loaded")
        table_loaded = sem("table_loaded")
        x_loaded = [sem(f"x_loaded{s}") for s in range(SLOTS)]
        single_loaded = [sem(f"single_loaded{g}") for g in range(GROUP)]
        stored = [sem(f"stored{s}") for s in range(SLOTS)]
        weights_selected = sem("weights_selected")
        product_ready = [sem(f"product_ready{k}") for k in range(BUFS)]
        sum_ready = [sem(f"sum_ready{k}") for k in range(BUFS)]

        block = ctx.enter_context(nc.Block())

        @block.sync
        def _(sp):
            def go_round(turn, first=False, last=False):
                for s in range(SLOTS):
                    if not first:
                        sp.wait_ge(stored[s], turn * DMA)
                    start = turn * per_turn + s * GROUP
                    if last and s == SLOTS - 1:
                        for g in range(GROUP):
                            sp.dma_start(ring[:, s, g], x_view[:, start + g, :]).then_inc(single_loaded[g], DMA)
                        continue
                    sp.dma_start(ring[:, s], x_view[:, bass.ds(start, GROUP), :]).then_inc(x_loaded[s], DMA)

            go_round(0, first=True)
            with sp.Fori(1, turns - 1) as turn:
                go_round(turn)
            go_round(turns - 1, last=True)

        @block.gpsimd
        def _(pool):
            pool.wait_ge(subjects_loaded, DMA)
            pool.wait_ge(table_loaded, DMA)

            def go_round(turn, first=False):
                for j in range(per_turn):
                    k = j % BUFS
                    subject = pool.value_load(subject_row[0:1, bass.ds(turn * per_turn + j, 1)],
                                              min_val=0, max_val=n_subjects - 1)
                    if not first or j >= BUFS:
                        pool.wait_ge(product_ready[k], turn * uses + j // BUFS)
                    nc.gpsimd.tensor_copy(selected[:, k, :],
                                          table[:, bass.ds(subject * mixed, mixed)]).then_inc(weights_selected, 1)

            go_round(0, first=True)
            with pool.Fori(1, turns) as turn:
                go_round(turn)

        @block.tensor
        def _(pe):
            def go_round(turn, first=False, last=False):
                for j in range(per_turn):
                    s, g, k = j // GROUP, j % GROUP, j % BUFS
                    if last and s == SLOTS - 1:
                        pe.wait_ge(single_loaded[g], DMA)
                    elif g == 0:
                        pe.wait_ge(x_loaded[s], turn * DMA + DMA)
                    pe.wait_ge(weights_selected, turn * per_turn + j + 1)
                    if not first or j >= BUFS:
                        pe.wait_ge(sum_ready[k], turn * uses + j // BUFS)
                    for n in range(banks):
                        cols = slice(n * BANK, (n + 1) * BANK)
                        product = nc.tensor.matmul(products[:, k, cols], selected[:, k, :], ring[:, s, g, cols],
                                                   start=True, stop=True)
                    product.then_inc(product_ready[k], 1)

            go_round(0, first=True)
            with pe.Fori(1, turns - 1) as turn:
                go_round(turn)
            go_round(turns - 1, last=True)

        @block.vector
        def _(dve):
            def go_round(turn, first=False):
                for j in range(per_turn):
                    s, g, k = j // GROUP, j % GROUP, j % BUFS
                    dve.wait_ge(product_ready[k], turn * uses + j // BUFS + 1)
                    nc.vector.tensor_tensor(ring[:, s, g, :], products[:, k, :], ring[:, s, g, :],
                                            ALU.add).then_inc(sum_ready[k], 1)

            go_round(0, first=True)
            with dve.Fori(1, turns) as turn:
                go_round(turn)

        @block.scalar
        def _(act):
            act.dma_start(subject_row[:], subjects.rearrange("(a b) -> a b", a=1)).then_inc(subjects_loaded, DMA)
            act.dma_start(table[:].rearrange("c (n d) -> c n d", n=n_subjects),
                          weights.rearrange("n c d -> c n d")).then_inc(table_loaded, DMA)

            def go_round(turn, first=False, last=False):
                for s in range(SLOTS):
                    start = turn * per_turn + s * GROUP
                    if last and s == SLOTS - 1:
                        for g in range(GROUP):
                            j = s * GROUP + g
                            act.wait_ge(sum_ready[j % BUFS], turn * uses + j // BUFS + 1)
                            act.dma_start(out_view[:, start + g, :], ring[:, s, g]).then_inc(stored[s], DMA)
                        continue
                    for j in range(s * GROUP, (s + 1) * GROUP):
                        act.wait_ge(sum_ready[j % BUFS], turn * uses + j // BUFS + 1)
                    act.dma_start(out_view[:, bass.ds(start, GROUP), :], ring[:, s]).then_inc(stored[s], DMA)

            go_round(0, first=True)
            with act.Fori(1, turns - 1) as turn:
                go_round(turn)
            go_round(turns - 1, last=True)
            for s in range(SLOTS - 1):
                act.wait_ge(stored[s], turns * DMA)
            act.wait_ge(stored[SLOTS - 1], (turns - 1 + GROUP) * DMA)


def kernel(x, itok_B_0_7, L0_cond_weights):
    import numpy as np
    import concourse.bacc as bacc
    from concourse.bass_utils import run_bass_kernel_spmd

    nc = bacc.Bacc("TRN2", target_bir_lowering=False, num_devices=1)
    inputs = {"x": np.ascontiguousarray(x), "subjects": np.ascontiguousarray(itok_B_0_7),
              "weights": np.ascontiguousarray(L0_cond_weights)}
    handles = [nc.dram_tensor(name, a.shape, mybir.dt.from_np(a.dtype), kind="ExternalInput").ap()
               for name, a in inputs.items()]
    out = nc.dram_tensor("out", inputs["x"].shape, F32, kind="ExternalOutput").ap()
    subject_mix_kernel(nc, *handles, out)
    result = run_bass_kernel_spmd(nc, [inputs], core_ids=[0])
    return result.results[0]["out"]
```
